# Optimizing a Trainium2 kernel written in Bass

```python
import numpy as np
import jax
import jax.numpy as jnp

def _softmax(x, axis=-1):
    return jax.nn.softmax(x, axis=axis)

def _gelu(x):
    return jax.nn.gelu(x, approximate=True)

def _silu(x):
    return jax.nn.silu(x)

def _sigmoid(x):
    return jax.nn.sigmoid(x)

def _layernorm(x, axis=-1, eps=1e-05):
    m = jnp.mean(x, axis=axis, keepdims=True)
    v = jnp.var(x, axis=axis, keepdims=True)
    return (x - m) / jnp.sqrt(v + eps)

def _scatter_add(tgt, idx, src, axis=0):
    return tgt.at[idx].add(src)

def _segment_sum(src, seg, n):
    return jax.ops.segment_sum(src, seg, n)
kernel_name = 'mk_gnn_resnorm_d4_gnn_r32_796942'

def setup_inputs(seed: int=0):
    np.random.seed(seed)
    _w = jnp.asarray

    def _rec_inputs():
        import jax
        import jax.numpy as jnp
        _gk = jax.random.key(seed)
        x = -0.0003713 + 1 * jax.random.normal(jax.random.fold_in(_gk, 1), (3125, 128), jnp.float32)
        _s = jax.random.randint(jax.random.fold_in(_gk, 2), (25000,), 0, 3125, jnp.int32)
        _d = jax.random.randint(jax.random.fold_in(_gk, 3), (25000,), 0, 3125, jnp.int32)
        _loop = jnp.arange(3125, dtype=jnp.int32)
        src = jnp.concatenate([_s, _d, _loop])
        dst = jnp.concatenate([_d, _s, _loop])
        _o = jnp.argsort(dst, stable=True)
        src = src[_o]
        dst = dst[_o]
        edge_type_16 = jax.random.randint(jax.random.fold_in(_gk, 13), (53125,), 0, 16, jnp.int32)
        edge_type_32 = jax.random.randint(jax.random.fold_in(_gk, 14), (53125,), 0, 32, jnp.int32)
        return (x, src, dst, edge_type_16, edge_type_32)
    x, src, dst, edge_type_16, edge_type_32 = _rec_inputs()

    def _L0_gnn_setup():
        import jax, jax.numpy as jnp
        import numpy as np
        N_NODES = 3125
        N_EDGES = 18750
        D_IN = 128
        D_OUT = 128
        N_REL = 16
        N_BASES = 2
        key = jax.random.key(seed)
        k1, k2, k3, k4, k5, k6 = jax.random.split(key, 6)
        x = jax.random.normal(k1, (N_NODES, D_IN), dtype=jnp.float32)
        edge_idx = jax.random.randint(k2, (2, N_EDGES), 0, N_NODES, dtype=jnp.int32)
        edge_type = jax.random.randint(k3, (N_EDGES,), 0, N_REL, dtype=jnp.int32)
        self_weight = jax.random.normal(k4, (D_IN, D_OUT), dtype=jnp.float32) * (2.0 / D_IN) ** 0.5
        bases = jax.random.normal(k5, (N_BASES, D_IN, D_OUT), dtype=jnp.float32) * (2.0 / (D_IN + D_OUT)) ** 0.5
        base_weights = jax.random.normal(k6, (N_REL, N_BASES), dtype=jnp.float32) * (2.0 / (N_REL + N_BASES)) ** 0.5
        return {'x': x, 'edge_idx': edge_idx, 'edge_type': edge_type, 'self_weight': self_weight, 'bases': bases, 'base_weights': base_weights}
    _L0_gnn_all = _L0_gnn_setup()
    _L0_gnn_in = {k: v for k, v in _L0_gnn_all.items() if k in ('self_weight', 'bases', 'base_weights')}
    del _L0_gnn_all

    def _L1_gnn_setup():
        import jax, jax.numpy as jnp
        import numpy as np
        N_NODES = 3125
        N_EDGES = 50000
        D = 128
        N_RELS = 32
        N_BASES = 4
        N_LAYERS = 2
        key = jax.random.key(seed)
        ks = jax.random.split(key, 8)
        feat = jax.random.normal(ks[0], (N_NODES, D), dtype=jnp.float32)
        src = jax.random.randint(ks[1], (N_EDGES,), 0, N_NODES, dtype=jnp.int32)
        dst = jax.random.randint(ks[2], (N_EDGES,), 0, N_NODES, dtype=jnp.int32)
        etype = jax.random.randint(ks[3], (N_EDGES,), 0, N_RELS, dtype=jnp.int32)
        scale = 1.0 / np.sqrt(D)
        basis = jax.random.normal(ks[4], (N_LAYERS, N_BASES, D, D), dtype=jnp.float32) * scale
        comp = jax.random.normal(ks[5], (N_LAYERS, N_RELS, N_BASES), dtype=jnp.float32)
        loop_w = jax.random.normal(ks[6], (N_LAYERS, D, D), dtype=jnp.float32) * scale
        bias = jnp.zeros((N_LAYERS, D), dtype=jnp.float32)
        return {'feat': feat, 'src': src, 'dst': dst, 'etype': etype, 'basis': basis, 'comp': comp, 'loop_w': loop_w, 'bias': bias}
    _L1_gnn_all = _L1_gnn_setup()
    _L1_gnn_in = {k: v for k, v in _L1_gnn_all.items() if k in ('basis', 'comp', 'loop_w', 'bias')}
    del _L1_gnn_all

    def _L2_gnn_setup():
        import jax, jax.numpy as jnp
        import numpy as np
        N_NODES = 3125
        N_EDGES = 20000
        IN_DIM = 128
        OUT_DIM = 128
        key = jax.random.key(seed)
        k1, k2, k3, k4 = jax.random.split(key, 4)
        x = jax.random.normal(k1, (N_NODES, IN_DIM), dtype=jnp.float32)
        edge_index = jax.random.randint(k2, (2, N_EDGES), 0, N_NODES, dtype=jnp.int64)
        bound = 1.0 / np.sqrt(IN_DIM)
        W = jax.random.uniform(k3, (OUT_DIM, IN_DIM), minval=-bound, maxval=bound, dtype=jnp.float32)
        b = jax.random.uniform(k4, (OUT_DIM,), minval=-bound, maxval=bound, dtype=jnp.float32)
        return {'x': x, 'edge_index': edge_index, 'W': W, 'b': b}
    _L2_gnn_all = _L2_gnn_setup()
    _L2_gnn_in = {k: v for k, v in _L2_gnn_all.items() if k in ('W', 'b')}
    del _L2_gnn_all

    def _L3_gnn_setup():
        import jax, jax.numpy as jnp
        import numpy as np
        N, E, IN_DIM, OUT_DIM, H = (50000, 25000, 128, 16, 8)
        key = jax.random.key(seed)
        ks = jax.random.split(key, 10)
        h = jax.random.normal(ks[0], (N, IN_DIM), dtype=jnp.float32)
        row = jnp.sort(jax.random.randint(ks[1], (E,), 0, N))
        col = jax.random.randint(ks[2], (E,), 0, N)
        s = 1.0 / np.sqrt(IN_DIM)
        Wq = jax.random.normal(ks[3], (IN_DIM, OUT_DIM * H), dtype=jnp.float32) * s
        Wk = jax.random.normal(ks[4], (IN_DIM, OUT_DIM * H), dtype=jnp.float32) * s
        Wv = jax.random.normal(ks[5], (IN_DIM, OUT_DIM * H), dtype=jnp.float32) * s
        bq = jnp.zeros((OUT_DIM * H,), jnp.float32)
        bk = jnp.zeros((OUT_DIM * H,), jnp.float32)
        bv = jnp.zeros((OUT_DIM * H,), jnp.float32)
        return {'h': h, 'Wq': Wq, 'bq': bq, 'Wk': Wk, 'bk': bk, 'Wv': Wv, 'bv': bv, 'row': row, 'col': col}
    _L3_gnn_all = _L3_gnn_setup()
    _L3_gnn_in = {k: v for k, v in _L3_gnn_all.items() if k in ('Wq', 'bq', 'Wk', 'bk', 'Wv', 'bv')}
    del _L3_gnn_all
    return {'x': x, 'src': src, 'dst': dst, 'edge_type_16': edge_type_16, 'edge_type_32': edge_type_32, 'L0_gnn_self_weight': _L0_gnn_in['self_weight'], 'L0_gnn_bases': _L0_gnn_in['bases'], 'L0_gnn_base_weights': _L0_gnn_in['base_weights'], 'L1_gnn_basis': _L1_gnn_in['basis'], 'L1_gnn_comp': _L1_gnn_in['comp'], 'L1_gnn_loop_w': _L1_gnn_in['loop_w'], 'L1_gnn_bias': _L1_gnn_in['bias'], 'L2_gnn_W': _L2_gnn_in['W'], 'L2_gnn_b': _L2_gnn_in['b'], 'L3_gnn_Wq': _L3_gnn_in['Wq'], 'L3_gnn_bq': _L3_gnn_in['bq'], 'L3_gnn_Wk': _L3_gnn_in['Wk'], 'L3_gnn_bk': _L3_gnn_in['bk'], 'L3_gnn_Wv': _L3_gnn_in['Wv'], 'L3_gnn_bv': _L3_gnn_in['bv']}

def reference(x, src, dst, edge_type_16, edge_type_32, L0_gnn_self_weight, L0_gnn_bases, L0_gnn_base_weights, L1_gnn_basis, L1_gnn_comp, L1_gnn_loop_w, L1_gnn_bias, L2_gnn_W, L2_gnn_b, L3_gnn_Wq, L3_gnn_bq, L3_gnn_Wk, L3_gnn_bk, L3_gnn_Wv, L3_gnn_bv):
    import jax
    import jax.numpy as jnp

    def _L0_gnn_ref(x, edge_idx, edge_type, self_weight, bases, base_weights):
        import jax, jax.numpy as jnp
        import numpy as np
        N_NODES = 3125
        N_EDGES = 18750
        D_IN = 128
        D_OUT = 128
        N_REL = 16
        N_BASES = 2
        heads = edge_idx[0]
        tails = edge_idx[1]
        gathered = x[heads]
        n_rel = base_weights.shape[0]

        def work_relation(acc, rel_inputs):
            rel, coef = rel_inputs
            rel_mask = (edge_type == rel)[:, None]
            msgs = jnp.where(rel_mask, gathered, 0.0)
            scattered = jnp.zeros_like(x).at[tails].add(msgs)
            w_rel = jnp.einsum('b,bio->io', coef, bases)
            return (acc + scattered @ w_rel, None)
        init = jnp.zeros((x.shape[0], bases.shape[2]), dtype=x.dtype)
        rel_out, _ = jax.lax.scan(work_relation, init, (jnp.arange(n_rel, dtype=edge_type.dtype), base_weights))
        return x @ self_weight + rel_out

    def _L1_gnn_ref(feat, src, dst, etype, basis, comp, loop_w, bias):
        import jax, jax.numpy as jnp
        import numpy as np
        N_NODES = 3125
        N_EDGES = 50000
        D = 128
        N_RELS = 32
        N_BASES = 4
        N_LAYERS = 2
        n_nodes = feat.shape[0]
        n_layers, n_bases = (basis.shape[0], basis.shape[1])
        h = feat
        for l in range(n_layers):
            h_src = h[src]
            c = comp[l][etype]
            msg = c[:, 0:1] * (h_src @ basis[l, 0])
            for b in range(1, n_bases):
                msg = msg + c[:, b:b + 1] * (h_src @ basis[l, b])
            agg = jax.ops.segment_sum(msg, dst, num_segments=n_nodes)
            h = jnp.tanh(agg + h @ loop_w[l] + bias[l])
        return h

    def _L2_gnn_ref(x, edge_index, W, b):
        import jax, jax.numpy as jnp
        import numpy as np
        N_NODES = 3125
        N_EDGES = 20000
        IN_DIM = 128
        OUT_DIM = 128
        src = edge_index[0]
        dst = edge_index[1]
        messages = x[src]
        agg = jax.ops.segment_sum(messages, dst, num_segments=x.shape[0])
        out = jax.nn.relu(agg @ W.T + b)
        return out

    def _L3_gnn_ref(h, Wq, bq, Wk, bk, Wv, bv, row, col):
        import jax, jax.numpy as jnp
        import numpy as np
        N, E, IN_DIM, OUT_DIM, H = (50000, 25000, 128, 16, 8)
        n = h.shape[0]
        scaling = OUT_DIM ** (-0.5)
        q = (h @ Wq + bq).reshape(n, OUT_DIM, H) * scaling
        k = (h @ Wk + bk).reshape(n, OUT_DIM, H)
        v = (h @ Wv + bv).reshape(n, OUT_DIM, H)
        s = jnp.einsum('edh,edh->eh', q[row], k[col])
        m = jax.ops.segment_max(s, row, num_segments=n)
        p = jnp.exp(s - m[row])
        z = jax.ops.segment_sum(p, row, num_segments=n)
        attn = p / z[row]
        out = jax.ops.segment_sum(attn[:, None, :] * v[col], row, num_segments=n)
        return out.reshape(n, -1)
    edge_index = jnp.stack([src, dst])
    x = _layernorm(x + _L0_gnn_ref(x, edge_index, edge_type_16, L0_gnn_self_weight, L0_gnn_bases, L0_gnn_base_weights), axis=-1)
    x = _layernorm(x + _L1_gnn_ref(x, src, dst, edge_type_32, L1_gnn_basis, L1_gnn_comp, L1_gnn_loop_w, L1_gnn_bias), axis=-1)
    x = _layernorm(x + _L2_gnn_ref(x, edge_index, L2_gnn_W, L2_gnn_b), axis=-1)
    x = _layernorm(x + _L3_gnn_ref(x, L3_gnn_Wq, L3_gnn_bq, L3_gnn_Wk, L3_gnn_bk, L3_gnn_Wv, L3_gnn_bv, src, dst), axis=-1)
    return x

_drawn_inputs = setup_inputs


def setup_inputs(seed=0):
    import zlib

    import numpy as np

    out = dict(_drawn_inputs(seed))
    spreads = {'L1_gnn_bias': (0.0, 0.1),
     'L3_gnn_bq': (0.0, 0.28),
     'L3_gnn_bk': (0.0, 0.8),
     'L3_gnn_bv': (0.0, 0.1)}
    factors = {}
    for name, (base, spread) in spreads.items():
        noise = np.random.default_rng([zlib.crc32(name.encode()), seed]).standard_normal(out[name].shape)
        drawn = base * np.exp(spread * noise) if base else spread * noise
        out[name] = jnp.asarray(drawn.astype(out[name].dtype))
    for name, factor in factors.items():
        out[name] = (out[name] * factor).astype(out[name].dtype)
    return out
```

```python
from contextlib import ExitStack

import concourse.bass as bass
from concourse import mybir

F32 = mybir.dt.float32
BF16 = mybir.dt.bfloat16
I32 = mybir.dt.int32
U16 = mybir.dt.uint16
U8 = mybir.dt.uint8
ALU = mybir.AluOpType
ACT = mybir.ActivationFunctionType
AX_X = mybir.AxisListType.X

P = 128
N = 3125
E = 53125
D = 128
NT = 25
NP = NT * P
EC = 416
EP = EC * P
HALF = EC // 2
R16, R32 = 16, 32
HEADS, HD = 8, 16
BLK = 32
FW = 12
F_SRC, F_C0, F_C1, F_C2, F_OK = 0, 1, 3, 7, 11
NCO = F_OK - F_C0
RING = 32
GRP = 8
WRING = 4
SCAP = E + NT + BLK + 3 * RING
DEGS = 64
PAD_DST = 4095
HIST = 64
PIECE = 16
BIG = 3.0e38
LOW = -1.0e30
EPS = 1e-5

C_ID = 0
C_TRIL = C_ID + P
C_TRIU = C_TRIL + P
C_I64 = C_TRIU + P
C_D64 = C_I64 + HIST
C_I32 = C_D64 + DEGS
C_REL = C_I32 + BLK
C_EPS = C_REL + 1
C_ONE = C_EPS + 1
C_NODE = C_ONE + P
C_W = C_NODE + NT


def constants():
    import numpy as np

    c = np.zeros((P, C_W), np.float32)
    r = np.arange(P)
    c[:, C_ID:C_ID + P] = np.eye(P)
    c[:, C_TRIL:C_TRIL + P] = r[:, None] < r[None, :]
    c[:, C_TRIU:C_TRIU + P] = r[:, None] > r[None, :]
    c[:, C_I64:C_I64 + HIST] = np.arange(HIST)
    c[:, C_D64:C_D64 + DEGS] = np.arange(DEGS)[::-1]
    c[:, C_I32:C_I32 + BLK] = np.arange(BLK)
    k = r % 64
    c[:, C_REL] = np.where(k < R16, k, np.where(k < R16 + R32, k - R16, -1))
    c[:, C_EPS] = EPS
    c[:, C_ONE:C_ONE + P] = 1.0
    c[:, C_NODE:C_NODE + NT] = r[:, None] * NT + np.arange(NT)[None, :]
    return c


def program(nc, a, out):
    ctx = ExitStack()
    pre = ExitStack()

    def sb(name, shape, dt=F32, stack=ctx):
        return stack.enter_context(nc.sbuf_tensor(name, shape, dt))

    def psum(name, shape, stack=ctx):
        return stack.enter_context(nc.psum_tensor(name, shape, F32))

    def sem(name):
        return ctx.enter_context(nc.semaphore(name))

    def dram(name, shape, dt=F32):
        return nc.dram_tensor(name, shape, dt).ap()

    def bc(ap, axis, n):
        ap = ap.unsqueeze(axis)
        return ap.broadcast_to([*ap.shape[:axis], n, *ap.shape[axis + 1:]])

    with ctx:
        rec_d = dram("rec_d", [EP + BLK, FW])
        hist_d = dram("hist_d", [2, HIST * HIST])
        node_d = dram("node_d", [NP, 4], I32)
        stream_d = [dram(f"stream{i}_d", [P // 2, SCAP, FW]) for i in range(2)]
        h_d = [a["x"]] + [dram(f"h{i}_d", [NP, D]) for i in range(1, 4)]
        kv_d = dram("kv_d", [NP, 2 * D])

        con = sb("con", [P, C_W])
        ident = con[:, C_ID:C_ID + P]
        ones_row = con[0:1, C_ONE:C_ONE + P]
        zrow = sb("zrow", [1, 512], BF16)
        w_self = sb("w_self", [P, D])
        w_bases = sb("w_bases", [P, 2, D])
        w_basis = sb("w_basis", [P, 2, 4, D])
        w_loop = sb("w_loop", [P, 2, D])
        w_lin = sb("w_lin", [P, D])
        w_qkv = sb("w_qkv", [P, 3 * D])
        b_rows = sb("b_rows", [1, 6 * D])
        node = sb("node", [P, NT, 4], I32)
        starts = sb("starts", [1, NT + 2], I32)
        X = sb("X", [P, NT, D])
        H = sb("H", [P, NT, D])

        flag = sb("flag", [1, 1], I32)

        deg = node[:, :, 2].bitcast(F32)
        ids = node[:, :, 0]

        s_ww = sem("s_ww")
        s_con, s_in, s_w, s_z = sem("s_con"), sem("s_in"), sem("s_w"), sem("s_z")
        s_v, s_typ, s_typfree = sem("s_v"), [sem("s_typ0"), sem("s_typ1")], sem("s_typfree")
        s_hi, s_hused, s_hist = sem("s_hi"), sem("s_hused"), sem("s_hist")
        s_oht, s_co, s_coused, s_rec, s_recd = sem("s_oht"), sem("s_co"), sem("s_coused"), sem("s_rec"), sem("s_recd")
        s_pe, s_hd, s_dn, s_pos = sem("s_pe"), sem("s_hd"), sem("s_dn"), sem("s_pos")
        s_nd, s_node, s_starts = sem("s_nd"), sem("s_node"), sem("s_starts")
        s_bi, s_bg, s_bm, s_bw, s_pool = sem("s_bi"), sem("s_bg"), sem("s_bm"), sem("s_bw"), sem("s_pool")

        src_s = sb("src_s", [P, EC], I32, pre)
        dst_s = sb("dst_s", [P, EC + 1], I32, pre)
        dhi = sb("dhi", [P, EC], I32, pre)
        dlo = sb("dlo", [P, EC], I32, pre)
        ohi = sb("ohi", [P, 2, PIECE, HIST], BF16, pre)
        olo = sb("olo", [P, 2, PIECE, HIST], BF16, pre)
        viol = sb("viol", [P, EC], F32, pre)
        viol1 = sb("viol1", [P, 1], F32, pre)
        typ = sb("typ", [P, 2, P // 8, HALF], I32, pre)
        oht = sb("oht", [P, P, HALF], BF16, pre)
        wrel = sb("wrel", [P, 2 * NCO], F32, pre)
        wsplit = sb("wsplit", [P, 2 * NCO, 3], BF16, pre)
        wrest = sb("wrest", [P, 2, 2 * NCO], F32, pre)
        rec = sb("rec", [P, EC, FW], F32, pre)
        recpad = sb("recpad", [BLK, FW], F32, pre)
        hdeg = sb("hdeg", [HIST, 4, HIST], F32, pre)
        hbase = sb("hbase", [HIST, 1], F32, pre)
        dn = sb("dn", [P, 2, NT], F32, pre)
        dmin = sb("dmin", [P, NT], F32, pre)
        ohb = sb("ohb", [P, DEGS, NT], F32, pre)
        zer = sb("zer", [P, DEGS * NT], F32, pre)
        rank = sb("rank", [P, DEGS, NT], F32, pre)
        cinc = sb("cinc", [P, 2, DEGS], F32, pre)
        other = sb("other", [P, DEGS], F32, pre)
        posf = sb("posf", [P, NT], F32, pre)
        pos = sb("pos", [P, NT], I32, pre)
        nrec = sb("nrec", [P, NT, 4], I32, pre)
        tmax = sb("tmax", [NT, 2], F32, pre)
        srow = sb("srow", [1, 2 * NT], F32, pre)
        zslots = sb("zslots", [P, 3 * RING * FW], F32, pre)
        bcur = sb("bcur", [P, 2], F32, pre)
        bidx = sb("bidx", [P, 1], I32, pre)
        bbuf = sb("bbuf", [P, BLK, FW], F32, pre)
        bmask = sb("bmask", [P, BLK], F32, pre)
        p_hist = psum("p_hist", [HIST, HIST], pre)
        p_small = psum("p_small", [P, 512], pre)
        p_co = psum("p_co", [P, 2, 512], pre)

        V_SUMS, V_ROWS = 7, 9

        def tile_slots(eng, t):
            lo = eng.value_load(starts[0:1, bass.ds(t, 1)], min_val=0, max_val=E + NT)
            hi = eng.value_load(starts[0:1, bass.ds(t + 1, 1)], min_val=1, max_val=E + NT)
            return lo, hi

        block = nc.Block()
        with block:
            @block.sync
            def _(sp):
                sp.dma_start(dst_s[:], a["dst"]).then_inc(s_in, 16)
                sp.dma_start(con[:], a["con"]).then_inc(s_con, 16)
                for i in range(8):
                    if i >= 2:
                        sp.wait_ge(s_typfree, i - 1)
                    for half in range(2):
                        for name, p0, n in (("t16", 0, R16), ("t32", R16, 64 - R16)):
                            m0 = i * (P // 8)
                            s = a[name][m0:m0 + P // 8, half * HALF:(half + 1) * HALF]
                            sp.dma_start(typ[64 * half + p0:64 * half + p0 + n, i % 2, :, :],
                                         s.partition_broadcast(n)).then_inc(s_typ[i % 2], 16)
                sp.dma_start(src_s[:], a["src"]).then_inc(s_w, 16)
                sp.dma_start(wrel[:], a["wrel"]).then_inc(s_w, 16)
                sp.wait_ge(s_v, V_ROWS)
                sp.dma_start(hist_d[0].rearrange("(a b) -> a b", b=HIST), hdeg[:, 0, :]).then_inc(s_hd, 16)
                sp.dma_start(hist_d[1].rearrange("(a b) -> a b", b=HIST), hdeg[:, 2, :]).then_inc(s_hd, 16)
                sp.wait_ge(s_hd, 32)
                sp.dma_start(dn[:, 0, :], hist_d[0, 0:NP].rearrange("(p t) -> p t", t=NT)).then_inc(s_dn, 16)
                sp.dma_start(dn[:, 1, :], hist_d[1, 0:NP].rearrange("(p t) -> p t", t=NT)).then_inc(s_dn, 16)
                sp.wait_ge(s_nd, 16 * NT)
                sp.dma_start(node[:], node_d.rearrange("(t p) w -> p t w", p=P)).then_inc(s_node, 16)
                sp.wait_ge(s_rec, 1)
                sp.dma_start(rec_d[0:EP].rearrange("(p c) w -> p c w", c=EC), rec[:]).then_inc(s_recd, 16)
                sp.dma_start(rec_d[EP:EP + BLK], recpad[:]).then_inc(s_recd, 16)
                sp.wait_ge(s_starts, 1)
                total = sp.value_load(starts[0:1, NT:NT + 1], min_val=NT, max_val=E + NT)
                for i in range(2):
                    sp.dma_start(stream_d[i][:, bass.ds(total, 3 * RING), :],
                                 zslots[64 * i:64 * i + 64].rearrange("p (s w) -> p s w", w=FW)).then_inc(s_bw, 16)
                items = sp.alloc_register("items")
                sp.reg_mov(items, 1)
                with sp.Fori(0, NT) as t:
                    lo, hi = tile_slots(sp, t)
                    with sp.Fori(lo, hi, BLK) as s0:
                        done = sp.snap(items, min_val=1, max_val=E)
                        sp.wait_ge(s_bw, done * 32)
                        sp.nop(nofuse=True)
                        sp.wait_ge(s_bm, done + 1)
                        for i in range(2):
                            sp.dma_start(stream_d[i][:, bass.ds(s0, BLK), :], bbuf[64 * i:64 * i + 64]).then_inc(s_bw, 16)
                        sp.reg_add(items, items, 1)
                done = sp.snap(items, min_val=1, max_val=E)
                sp.wait_ge(s_bw, done * 32)
                sp.nop(nofuse=True)

            @block.vector
            def _(dve):
                count = [0]

                def link(ins):
                    count[0] += 1
                    ins.then_inc(s_v, 1)
                    dve.wait_ge(s_v, count[0])

                dve.memset(zrow[:], 0.0).then_inc(s_z, 1)
                link(dve.memset(hdeg[:], 0.0))
                dve.sem_inc(s_hused, 2)
                dve.wait_ge(s_in, 16)
                link(dve.tensor_scalar(dhi[:], dst_s[:, 0:EC], 6, None, ALU.logical_shift_right))
                link(dve.tensor_scalar(dlo[:], dst_s[:, 0:EC], 63, None, ALU.bitwise_and))
                dve.wait_ge(s_con, 16)
                with dve.Fori(0, EC // PIECE // 2) as i:
                    for half in range(2):
                        dve.wait_ge(s_hused, i * 2 + half + 1)
                        dve.tensor_tensor(ohi[:, half], bc(dhi[:, bass.ds(i * (2 * PIECE) + half * PIECE, PIECE)], 2, HIST),
                                          bc(con[:, C_I64:C_I64 + HIST], 1, PIECE), ALU.is_equal)
                        dve.tensor_tensor(olo[:, half], bc(dlo[:, bass.ds(i * (2 * PIECE) + half * PIECE, PIECE)], 2, HIST),
                                          bc(con[:, C_I64:C_I64 + HIST], 1, PIECE), ALU.is_equal).then_inc(s_hi, 1)
                link(dve.tensor_tensor(viol[:], dst_s[:, 0:EC], dst_s[:, 1:EC + 1], ALU.is_gt))
                link(dve.tensor_reduce(viol1[:], viol[:], AX_X, ALU.max))
                dve.wait_ge(s_hist, 1)
                link(dve.tensor_copy(hdeg[:, 0, :], p_hist[:]))
                link(dve.tensor_tensor_scan(hdeg[:, 1, :], hdeg[:, 3, :], hdeg[:, 0, :], 0.0, ALU.add, ALU.add))
                dve.wait_ge(s_pe, 1)
                link(dve.tensor_tensor(hdeg[:, 2, :], hdeg[:, 1, :], hdeg[:, 0, :], ALU.subtract))
                link(dve.tensor_scalar(hdeg[:, 2, :], hdeg[:, 2, :], p_small[0:HIST, 0:1], None, ALU.add))
                assert count[0] == V_ROWS
                dve.tensor_scalar(flag[:], p_small[0:1, 1:2], 1.0, None, ALU.min).then_inc(s_z, 1)
                for i in range(8):
                    dve.wait_ge(s_typ[i % 2], 64 * (i // 2 + 1))
                    m0 = i * (P // 8)
                    dve.tensor_scalar(oht[:, m0:m0 + P // 8, :], typ[:, i % 2], con[:, C_REL:C_REL + 1], None,
                                      ALU.is_equal).then_inc(s_typfree, 1)
                dve.wait_ge(s_w, 32)
                link(dve.tensor_copy(wsplit[:, :, 0], wrel[:]))
                link(dve.tensor_tensor(wrest[:, 0], wrel[:], wsplit[:, :, 0], ALU.subtract))
                link(dve.tensor_copy(wsplit[:, :, 1], wrest[:, 0]))
                link(dve.tensor_tensor(wrest[:, 1], wrest[:, 0], wsplit[:, :, 1], ALU.subtract))
                dve.tensor_copy(wsplit[:, :, 2], wrest[:, 1]).then_inc(s_oht, 1)
                dve.tensor_copy(rec[:, :, F_SRC].bitcast(I32), src_s[:])
                dve.memset(rec[:, :, F_OK], 1.0)
                dve.memset(zslots[:], 0.0)
                dve.memset(recpad[:], 0.0)
                link(dve.memset(zer[:], 0.0))
                dve.wait_ge(s_dn, 32)
                link(dve.tensor_scalar(dmin[:], dn[:, 0, :], float(DEGS - 1), None, ALU.min))
                link(dve.tensor_tensor(ohb[:], bc(dmin[:], 1, DEGS), bc(con[:, C_D64:C_D64 + DEGS], 2, NT), ALU.is_equal))
                link(dve.tensor_tensor_scan(rank[:].rearrange("p b t -> p (b t)"), zer[:],
                                            ohb[:].rearrange("p b t -> p (b t)"), 0.0, ALU.add, ALU.add))
                dve.memset(cinc[:, 1, 0:1], 0.0)
                dve.tensor_copy(cinc[:, 0, :], rank[:, :, NT - 1])
                link(dve.tensor_copy(cinc[:, 1, 1:DEGS], rank[:, 0:DEGS - 1, NT - 1]))
                dve.sem_inc(s_pos, 1)
                dve.wait_ge(s_pe, 2)
                link(dve.tensor_copy(other[:], p_small[:, 64:64 + DEGS]))
                link(dve.tensor_tensor(rank[:], rank[:], bc(other[:], 2, NT), ALU.add))
                link(dve.tensor_tensor(rank[:], rank[:], ohb[:], ALU.mult))
                link(dve.tensor_reduce(posf[:], rank[:].rearrange("p b t -> p t b"), AX_X, ALU.add))
                dve.tensor_scalar(pos[:], posf[:], -1.0, None, ALU.add)
                dve.tensor_copy(nrec[:, :, 0], con[:, C_NODE:C_NODE + NT])
                dve.tensor_scalar(nrec[:, :, 1], dn[:, 1, :], float(FW), None, ALU.mult)
                dve.tensor_copy(nrec[:, :, 2].bitcast(F32), dn[:, 0, :])
                dve.memset(nrec[:, :, 3], 0).then_inc(s_pos, 1)
                with dve.Fori(0, HALF // 16) as i:
                    for half in range(2):
                        dve.wait_ge(s_co, i * 2 + half + 1)
                        c0 = i * 16 + half * 8
                        parts = p_co[:, half, 0:8 * 6 * NCO].rearrange("p (c k f s) -> p c k f s", k=2, f=NCO, s=3)
                        for k in range(2):
                            last = dve.tensor_reduce(rec[:, bass.ds(c0 + k * HALF, 8), F_C0:F_OK], parts[:, :, k],
                                                     AX_X, ALU.add)
                        last.then_inc(s_coused, 1)
                link(dve.memset(tmax[:], 0.0))
                dve.sem_inc(s_rec, 1)
                dve.wait_ge(s_pe, 3)
                link(dve.tensor_reduce(tmax[:, 0:1], p_small[0:NT, 128:256], AX_X, ALU.max))
                link(dve.tensor_scalar(tmax[:, 1:2], tmax[:, 0:1], 1.0, None, ALU.max))
                dve.sem_inc(s_pos, 1)
                dve.wait_ge(s_pe, 4)
                link(dve.tensor_copy(srow[:, 0:NT], p_small[0:1, 256:256 + NT]))
                link(dve.tensor_tensor_scan(srow[:, NT:2 * NT], zer[0:1, 0:NT], srow[:, 0:NT], 0.0, ALU.add, ALU.add))
                dve.memset(starts[:, 0:1], 0)
                link(dve.tensor_copy(starts[:, 1:NT + 1], srow[:, NT:2 * NT]))
                link(dve.tensor_scalar(starts[:, NT + 1:NT + 2], starts[:, NT:NT + 1], -1.0, None, ALU.add))
                link(dve.tensor_scalar(starts[:, NT + 1:NT + 2], starts[:, NT + 1:NT + 2], -RING, None, ALU.bitwise_and))
                dve.sem_inc(s_starts, 1)
                items = dve.alloc_register("items_v")
                dve.reg_mov(items, 0)
                dve.sem_inc(s_bm, 1)
                base = count[0]
                with dve.Fori(0, NT) as t:
                    lo, hi = tile_slots(dve, t)
                    first = dve.snap(items, min_val=0, max_val=E)
                    dve.wait_ge(s_bm, first + 1)
                    dve.tensor_copy(bcur[:, 0:1], node[:, bass.ds(t, 1), 1])
                    dve.tensor_copy(bcur[:, 1:2], node[:, bass.ds(t, 1), 2].bitcast(F32)).then_inc(s_bi, 1)
                    with dve.Fori(lo, hi, BLK) as s0:
                        it = dve.snap(items, min_val=0, max_val=E)
                        dve.wait_ge(s_bi, it * 3 + t + 1)
                        dve.tensor_scalar(bmask[:], con[:, C_I32:C_I32 + BLK], bcur[:, 1:2], None, ALU.is_lt)
                        dve.tensor_scalar(bidx[:], bcur[:, 0:1], float(EP * FW), None, ALU.min).then_inc(s_bi, 1)
                        dve.wait_ge(s_bi, it * 3 + t + 2)
                        dve.tensor_scalar(bcur[:, 0:1], bcur[:, 0:1], float(BLK * FW), None, ALU.add)
                        dve.tensor_scalar(bcur[:, 1:2], bcur[:, 1:2], -float(BLK), None, ALU.add).then_inc(s_bi, 1)
                        dve.wait_ge(s_bg, it * 16 + 16)
                        dve.tensor_tensor(bbuf[:, :, 1:FW], bbuf[:, :, 1:FW], bc(bmask[:], 2, FW - 1),
                                          ALU.mult).then_inc(s_bi, 1)
                        dve.wait_ge(s_bi, it * 3 + t + 4)
                        dve.sem_inc(s_bm, 1)
                        dve.reg_add(items, items, 1)

            @block.gpsimd
            def _(pool):
                pool.wait_ge(s_pos, 2)
                for t in range(NT):
                    pool.indirect_dma_start(node_d, bass.IndirectOffsetOnAxis(ap=pos[:, t:t + 1], axis=0),
                                            nrec[:, t, :], None).then_inc(s_nd, 16)
                pool.wait_ge(s_recd, 32)
                items = pool.alloc_register("items_p")
                pool.reg_mov(items, 0)
                pool.wait_ge(s_starts, 1)
                with pool.Fori(0, NT) as t:
                    lo, hi = tile_slots(pool, t)
                    with pool.Fori(lo, hi, BLK) as s0:
                        it = pool.snap(items, min_val=0, max_val=E)
                        pool.wait_ge(s_bi, it * 3 + t + 2)
                        pool.wait_ge(s_bw, it * 32 + 32)
                        pool.nop(nofuse=True)
                        pool.indirect_dma_start(bbuf[:].rearrange("p s w -> p (s w)"), None,
                                                rec_d.rearrange("e w -> (e w)").rearrange("(a b) -> a b", b=BLK * FW),
                                                bass.IndirectOffsetOnAxis(ap=bidx[:], axis=1)).then_inc(s_bg, 16)
                        pool.reg_add(items, items, 1)

            @block.tensor
            def _(pe):
                pe.wait_ge(s_z, 1)
                pe.matmul(p_hist[:], zrow[0:1, 0:HIST], zrow[0:1, 0:HIST], start=True, stop=False)
                with pe.Fori(0, EC // PIECE // 2) as i:
                    for half in range(2):
                        pe.wait_ge(s_hi, i * 2 + half + 1)
                        for c in range(PIECE):
                            last = pe.matmul(p_hist[:], ohi[:, half, c, :], olo[:, half, c, :], start=False, stop=False)
                        last.then_inc(s_hused, 1)
                pe.matmul(p_hist[:], zrow[0:1, 0:HIST], zrow[0:1, 0:HIST], start=False, stop=True).then_inc(s_hist, 1)
                pe.wait_ge(s_v, V_SUMS)
                pe.matmul(p_small[0:HIST, 0:1], con[0:HIST, C_TRIL:C_TRIL + HIST], hdeg[:, 1, HIST - 1:HIST],
                          start=True, stop=True)
                pe.matmul(p_small[0:1, 1:2], viol1[:], con[:, C_ONE:C_ONE + 1], start=True, stop=True).then_inc(s_pe, 1)
                pe.wait_ge(s_pos, 1)
                pe.matmul(p_small[:, 64:64 + DEGS], con[:, C_TRIL:C_TRIL + P], cinc[:, 0, :], start=True, stop=False)
                pe.matmul(p_small[:, 64:64 + DEGS], con[:, C_TRIU:C_TRIU + P], cinc[:, 1, :], start=False,
                          stop=True).then_inc(s_pe, 1)
                pe.wait_ge(s_typfree, 8)
                pe.wait_ge(s_oht, 1)
                pe.sem_inc(s_coused, 2)
                with pe.Fori(0, HALF // 16) as i:
                    for half in range(2):
                        pe.wait_ge(s_coused, i * 2 + half + 1)
                        for j in range(8):
                            c = i * 16 + half * 8 + j
                            last = pe.matmul(p_co[:, half, j * 6 * NCO:(j + 1) * 6 * NCO], oht[:, :, bass.ds(c, 1)].rearrange("p m o -> p (m o)"),
                                             wsplit[:].rearrange("p f s -> p (f s)"), start=True, stop=True)
                        last.then_inc(s_co, 1)
                pe.wait_ge(s_node, 16)
                pe.transpose(p_small[0:NT, 128:256], deg, ident).then_inc(s_pe, 1)
                pe.wait_ge(s_pos, 3)
                pe.matmul(p_small[0:1, 256:256 + NT], tmax[:, 1:2], con[0:NT, 0:NT], start=True,
                          stop=True).then_inc(s_pe, 1)

            @block.scalar
            def _(act):
                for w, name in ((w_self, "w_self"), (w_bases, "w_bases"), (w_basis, "w_basis"), (w_loop, "w_loop"),
                                (w_lin, "w_lin"), (w_qkv, "w_qkv"), (b_rows, "b_rows")):
                    act.dma_start(w[:], a[name]).then_inc(s_ww, 16)
                act.wait_ge(s_ww, 16 * 7)
                act.wait_ge(s_node, 16)
                act.wait_ge(s_starts, 1)
        pre.close()
        layers(nc, ctx, out, con, zrow, w_self, w_bases, w_basis, w_loop, w_lin, w_qkv, b_rows, node, starts, X, H,
               stream_d, h_d, kv_d, tile_slots)


def layers(nc, ctx, out, con, zrow, w_self, w_bases, w_basis, w_loop, w_lin, w_qkv, b_rows, node, starts, X, H,
           stream_d, h_d, kv_d, tile_slots):
    def sb(name, shape, dt=F32):
        return ctx.enter_context(nc.sbuf_tensor(name, shape, dt))

    def psum(name, shape):
        return ctx.enter_context(nc.psum_tensor(name, shape, F32))

    def sem(name):
        return ctx.enter_context(nc.semaphore(name))

    def bc(ap, axis, n):
        ap = ap.unsqueeze(axis)
        return ap.broadcast_to([*ap.shape[:axis], n, *ap.shape[axis + 1:]])

    ident = con[:, C_ID:C_ID + P]
    ones_row = con[0:1, C_ONE:C_ONE + P]

    sl = sb("sl", [P, RING, FW])
    G = sb("G", [P, RING, 2 * D])
    W = sb("W", [P, WRING, 4, D])
    agg_s = sb("agg_s", [P, 4 * D])
    x_s = sb("x_s", [P, D])
    tr_s = sb("tr_s", [P, 5 * D])
    y = sb("y", [P, D])
    act_o = sb("act_o", [P, D])
    bn6 = sb("bn6", [P, 6])
    mv = sb("mv", [P, 2])
    std = sb("std", [P, 1])
    rstd = sb("rstd", [P, 1])
    bn6s = sb("bn6s", [P, NT, 6])
    mvs = sb("mvs", [P, NT, 2])
    stds = sb("stds", [P, NT])
    rstds = sb("rstds", [P, NT])
    KV = sb("KV", [P, NT, 2 * D])
    x3_s = sb("x3_s", [P, D])
    x3t_s = sb("x3t_s", [P, D])
    agg = psum("agg", [P, 2, 4 * D])
    tr = psum("tr", [P, 2, 4 * D])
    o = psum("o", [P, 4 * D])
    x3t = psum("x3t", [P, 4 * D])
    qkv = psum("qkv", [P, 4 * D])

    s_sl = [sem(f"s_sl{h}") for h in range(RING // GRP)]
    s_arr = [sem(f"s_arr{k}") for k in range(RING)]

    class Sems:

        def __init__(self, n):
            self.n = n
            self.arrived = sem(f"arrived{n}")
            self.used = sem(f"used{n}")
            self.w_dve, self.w_act = sem(f"w_dve{n}"), sem(f"w_act{n}")
            self.agg_ready = sem(f"agg_ready{n}")
            self.agg_copied = sem(f"agg_copied{n}")
            self.tr_ready, self.tr_copied = sem(f"tr_ready{n}"), sem(f"tr_copied{n}")
            self.o_ready = sem(f"o_ready{n}")
            self.act_o = sem(f"act_o{n}")
            self.ln = sem(f"ln{n}")
            self.std = sem(f"std{n}")
            self.done = sem(f"done{n}")
            self.stored = sem(f"stored{n}")

    def rounds(eng, slots, phases):
        last = max([d for d, _ in phases], default=0)

        def one(r):
            if slots and not (isinstance(r, int) and r >= NT):
                slots(r)
            for d, f in phases:
                if not isinstance(r, int) or 0 <= r - d < NT:
                    f(r - d)

        for r in range(last):
            one(r)
        with eng.Fori(last, NT) as r:
            one(r)
        for r in range(NT, NT + last):
            one(r)

    def wait_nth(eng, s, n):
        if not (isinstance(n, int) and n == 0):
            eng.wait_ge(s, n)

    def at(buf, t):
        return buf[:, t, :]

    def load_records(sp, m, used, last):
        def load(s0, half):
            for i in range(2):
                sp.dma_start(sl[64 * i:64 * i + 64, half * GRP:(half + 1) * GRP, :],
                             stream_d[i][:, bass.ds(s0 + half * GRP, GRP), :]).then_inc(s_sl[half], 16)

        def pass_on(s0, half):
            for k in range(half * GRP, (half + 1) * GRP):
                sp.wait_ge(s_arr[k], before + s0 * 16 // RING + 16)
                sp.sem_inc(m.arrived, 1)

        before = (last + RING) * 16 // RING * m.n
        groups = RING // GRP
        for q in range(groups - 1):
            load(0, q)
        with sp.Fori(0, last, RING) as s0:
            for q in range(groups):
                pass_on(s0, q)
                ahead = s0 if q == 0 else s0 + RING
                place = (q - 1) % groups
                for u, steps in used:
                    sp.wait_ge(u, (ahead + (place + 1) * GRP) * steps)
                sp.nop(nofuse=True)
                load(ahead, place)
        pass_on(last, 0)
        for u, steps in used:
            sp.wait_ge(u, (last + RING) * steps)
        sp.nop(nofuse=True)
        load(last, groups - 1)
        for q in range(1, groups):
            pass_on(last, q)

    def gather(pool, m, used, table, width, total):
        before = (last_group(pool) + RING) * 32 // RING * m.n
        with pool.Fori(0, total, RING) as s0:
            for half in range(RING // GRP):
                pool.wait_ge(s_sl[half], before + s0 * 32 // RING + 32)
                for k in range(half * GRP, (half + 1) * GRP):
                    for u, steps in used:
                        pool.wait_ge(u, (s0 + k + 1) * steps)
                    pool.nop(nofuse=True)
                    pool.indirect_dma_start(G[:, k, 0:width], None, table,
                                            bass.IndirectOffsetOnAxis(ap=sl[:, k, 0:1].bitcast(I32), axis=0)
                                            ).then_inc(s_arr[k], 16)

    def total_slots(eng):
        return eng.value_load(starts[0:1, NT:NT + 1], min_val=NT, max_val=E + NT)

    def last_group(eng):
        return eng.value_load(starts[0:1, NT + 1:NT + 2], min_val=0, max_val=E + NT)

    def scatter(pool, m, done, buf, table):
        for t in range(NT):
            pool.wait_ge(done, t + 1)
            pool.indirect_dma_start(table, bass.IndirectOffsetOnAxis(ap=node[:, t, 0:1], axis=0), buf[:, t, :],
                                    None).then_inc(m.stored, 16)
        pool.wait_ge(m.stored, 16 * NT)

    def normalise(dve, m, t, write_y):
        wait_nth(dve, m.done, t)
        write_y().then_inc(m.ln, 1)
        dve.wait_ge(m.ln, t * 4 + 4)
        dve.bn_stats(bn6[:], y[:]).then_inc(m.ln, 1)
        dve.wait_ge(m.ln, t * 4 + 5)
        dve.nop(nofuse=True)
        dve.bn_aggr(mv[:], bn6[:]).then_inc(m.ln, 1)
        dve.wait_ge(m.std, t + 1)
        dve.reciprocal(rstd[:], std[:]).then_inc(m.ln, 1)
        dve.wait_ge(m.ln, t * 4 + 7)
        dve.tensor_scalar(at(X, t), y[:], mv[:, 0:1], rstd[:], ALU.subtract, ALU.mult).then_inc(m.done, 1)

    def residual(dve, m, t, write):
        write(at(X, t)).then_inc(m.ln, 1)
        dve.wait_ge(m.ln, t * 2 + 2)
        dve.bn_stats(bn6s[:, t, :], at(X, t)).then_inc(m.ln, 1)

    def normalise_all(dve, m):
        dve.wait_ge(m.ln, NT * 2 + 1)
        for t in range(NT):
            last = dve.bn_aggr(mvs[:, t, :], bn6s[:, t, :])
        last.then_inc(m.ln, 1)
        dve.wait_ge(m.std, 1)
        dve.reciprocal(rstds[:], stds[:]).then_inc(m.ln, 1)
        dve.wait_ge(m.ln, NT * 2 + 3)
        for t in range(NT):
            dve.tensor_scalar(X[:, t, :], X[:, t, :], mvs[:, t, 0:1], rstds[:, t:t + 1], ALU.subtract,
                              ALU.mult).then_inc(m.done, 1)

    def deviation_all(act, m):
        act.wait_ge(m.ln, NT * 2 + 2)
        act.activation(stds[:], mvs[:, :, 1], ACT.Sqrt, bias=con[:, C_EPS:C_EPS + 1], scale=1.0).then_inc(m.std, 1)

    def deviation(act, m, t):
        act.wait_ge(m.ln, t * 4 + 6)
        act.activation(std[:], mv[:, 1:2], ACT.Sqrt, bias=con[:, C_EPS:C_EPS + 1], scale=1.0).then_inc(m.std, 1)

    def sum_layer(n, table, nb, f0, weights, self_term, bias, kind):
        m = Sems(n)
        nd = min(nb, 2)
        width = nb * D
        ntr = nb + (self_term is not None)
        x_in = H if kind == "tanh_res" else X

        def p_slots(pe):
            def f(t):
                lo, hi = tile_slots(pe, t)
                pe.wait_ge(m.agg_copied, t + 1)
                pe.matmul(agg[:, t % 2, 0:width], zrow[0:1, 0:P], zrow[0:1, 0:width], start=True, stop=False)
                with pe.Fori(lo, hi) as g:
                    if nb > nd:
                        pe.wait_ge(m.w_act, g + 1)
                    pe.wait_ge(m.w_dve, g + 1)
                    pe.matmul(agg[:, t % 2, 0:width], ident, W[:, g % WRING, 0:nb, :], start=False,
                              stop=False).then_inc(m.used, 1)
                pe.matmul(agg[:, t % 2, 0:width], zrow[0:1, 0:P], zrow[0:1, 0:width], start=False,
                          stop=True).then_inc(m.agg_ready, 1)
            return f

        def p_transpose(pe):
            def f(t):
                pe.wait_ge(m.agg_copied, t + 3)
                wait_nth(pe, m.tr_copied, t)
                for b in range(nb):
                    last = pe.transpose(tr[:, 0, b * D:(b + 1) * D], agg_s[:, b * D:(b + 1) * D], ident)
                if self_term is not None:
                    last = pe.transpose(tr[:, 1, 0:D], x_s[:], ident)
                last.then_inc(m.tr_ready, 1)
            return f

        def p_product(pe):
            def f(t):
                pe.wait_ge(m.tr_copied, t + 1)
                if kind == "tanh":
                    wait_nth(pe, m.done, t)
                elif kind == "tanh_res":
                    wait_nth(pe, m.act_o, t)
                else:
                    wait_nth(pe, m.ln, t * 4)
                rows = [(tr_s[:, b * D:(b + 1) * D], weights[b]) for b in range(nb)]
                if self_term is not None:
                    rows.append((tr_s[:, nb * D:(nb + 1) * D], self_term))
                if bias is not None:
                    rows.append((ones_row, bias))
                for i, (l, r) in enumerate(rows):
                    last = pe.matmul(o[:, 0:D], l, r, start=(i == 0), stop=(i == len(rows) - 1))
                last.then_inc(m.o_ready, 1)
            return f

        def a_slots(act):
            def f(t):
                lo, hi = tile_slots(act, t)
                with act.Fori(lo, hi) as g:
                    act.wait_ge(m.arrived, g + 1)
                    act.wait_ge(m.used, g + 1 + RING - WRING)
                    act.nop(nofuse=True)
                    for b in range(nd, nb):
                        last = act.activation(W[:, g % WRING, b, :], G[:, g % RING, 0:D], ACT.Copy,
                                              scale=sl[:, g % RING, f0 + b:f0 + b + 1])
                    last.then_inc(m.w_act, 1)
            return f

        def a_sums(act):
            def f(t):
                act.wait_ge(m.agg_ready, t + 1)
                wait_nth(act, m.tr_ready, t)
                if self_term is not None:
                    act.activation(x_s[:], at(x_in, t), ACT.Copy)
                act.activation(agg_s[:, 0:width], agg[:, t % 2, 0:width], ACT.Copy).then_inc(m.agg_copied, 1)
            return f

        def a_transposed(act):
            def f(t):
                act.wait_ge(m.tr_ready, t + 1)
                wait_nth(act, m.o_ready, t)
                last = act.activation(tr_s[:, 0:width], tr[:, 0, 0:width], ACT.Copy)
                if self_term is not None:
                    last = act.activation(tr_s[:, width:width + D], tr[:, 1, 0:D], ACT.Copy)
                last.then_inc(m.tr_copied, 1)
            return f

        def a_result(act):
            def f(t):
                if kind in ("tanh", "tanh_res"):
                    act.wait_ge(m.o_ready, t + 1)
                    if kind == "tanh":
                        act.activation(at(H, t), o[:, 0:D], ACT.Tanh).then_inc(m.done, 1)
                        return
                    wait_nth(act, m.ln, t * 2)
                    act.activation(act_o[:], o[:, 0:D], ACT.Tanh).then_inc(m.act_o, 1)
                else:
                    deviation(act, m, t)
            return f

        def v_slots(dve):
            def f(t):
                lo, hi = tile_slots(dve, t)
                with dve.Fori(lo, hi) as g:
                    dve.wait_ge(m.arrived, g + 1)
                    dve.wait_ge(m.used, g + 1 + RING - WRING)
                    dve.tensor_tensor(W[:, g % WRING, 0:nd, :], bc(G[:, g % RING, 0:D], 1, nd),
                                      bc(sl[:, g % RING, f0:f0 + nd], 2, D), ALU.mult).then_inc(m.w_dve, 1)
            return f

        def v_result(dve):
            def f(t):
                if kind == "tanh_res":
                    dve.wait_ge(m.act_o, t + 1)
                    residual(dve, m, t, lambda x: dve.tensor_tensor(x, act_o[:], x, ALU.add))
                else:
                    dve.wait_ge(m.o_ready, t + 1)
                    if kind == "res":
                        normalise(dve, m, t, lambda: dve.tensor_tensor(y[:], o[:, 0:D], at(X, t), ALU.add))
                    else:
                        normalise(dve, m, t, lambda: dve.scalar_tensor_tensor(y[:], o[:, 0:D], 0.0, at(X, t),
                                                                              ALU.max, ALU.add))
            return f

        if kind == "relu_res":
            x3_copied, x3_tr, x3t_copied, qkv_ready, kv_done = (sem(f"{k}{n}") for k in (
                "x3_copied", "x3_tr", "x3t_copied", "qkv_ready", "kv_done"))

            def a_x3(t):
                act = nc.scalar
                act.wait_ge(m.done, t + 1)
                wait_nth(act, x3_tr, t)
                act.nop(nofuse=True)
                act.activation(x3_s[:], at(X, t), ACT.Copy).then_inc(x3_copied, 1)

            def a_x3t(t):
                act = nc.scalar
                act.wait_ge(x3_tr, t + 1)
                wait_nth(act, qkv_ready, t)
                act.activation(x3t_s[:], x3t[:, 0:D], ACT.Copy).then_inc(x3t_copied, 1)

            def a_qkv(t):
                act = nc.scalar
                act.wait_ge(qkv_ready, t + 1)
                act.nop(nofuse=True)
                act.activation(at(H, t), qkv[:, 0:D], ACT.Copy, scale=float(HD) ** -0.5)
                act.activation(at(KV, t), qkv[:, D:3 * D], ACT.Copy).then_inc(kv_done, 1)

            def p_x3(t):
                pe = nc.tensor
                pe.wait_ge(x3_copied, t + 1)
                wait_nth(pe, x3t_copied, t)
                pe.transpose(x3t[:, 0:D], x3_s[:], ident).then_inc(x3_tr, 1)

            def p_qkv(t):
                pe = nc.tensor
                pe.wait_ge(x3t_copied, t + 1)
                wait_nth(pe, kv_done, t)
                pe.matmul(qkv[:, 0:3 * D], x3t_s[:], w_qkv[:], start=True, stop=False)
                pe.matmul(qkv[:, 0:3 * D], ones_row, b_rows[:, 3 * D:6 * D], start=False, stop=True).then_inc(qkv_ready, 1)

        block = nc.Block()
        with block:
            @block.sync
            def _(sp):
                load_records(sp, m, [(m.used, 1)], last_group(sp))

            @block.gpsimd
            def _(pool):
                gather(pool, m, [(m.used, 1)], table, D, total_slots(pool))
                if kind == "relu_res":
                    scatter(pool, m, kv_done, KV, kv_d)
                else:
                    scatter(pool, m, m.done, H if kind == "tanh" else X, h_d[n + 1])

            @block.tensor
            def _(pe):
                pe.sem_inc(m.used, RING)
                phases = [(1, p_transpose(pe)), (2, p_product(pe))]
                if kind == "relu_res":
                    phases += [(4, p_x3), (5, p_qkv)]
                rounds(pe, p_slots(pe), phases)

            @block.vector
            def _(dve):
                dve.sem_inc(m.ln, 1 if kind == "tanh_res" else 3)
                rounds(dve, v_slots(dve), [] if kind == "tanh" else [(3, v_result(dve))])
                if kind == "tanh_res":
                    normalise_all(dve, m)

            @block.scalar
            def _(act):
                act.preload_act_table(ACT.Tanh if kind in ("tanh", "tanh_res") else ACT.Sqrt)
                act.sem_inc(m.agg_copied, 2)
                phases = [(1, a_sums(act)), (2, a_transposed(act)), (3, a_result(act))]
                if kind == "relu_res":
                    phases += [(4, a_x3), (5, a_x3t), (6, a_qkv)]
                rounds(act, a_slots(act) if nb > nd else None, phases)
                if kind == "tanh_res":
                    deviation_all(act, m)

    def block_end(eng, reg, s0, hi):
        eng.reg_alu(reg, s0 + BLK, hi, ALU.min)
        return eng.snap(reg, min_val=1, max_val=E + NT)

    def place(g, s0):
        return (g - s0).with_bounds(min_val=0, max_val=BLK - 1)

    def attention_layer(n):
        m = Sems(n)
        k_step = sem("k_step")
        v_copied = sem("v_copied")
        sm = sem("sm")
        ex_done = sem("ex_done")
        added = sem("added")
        fin = sem("fin")
        STEPS, FINS = 13, 4

        prod = W[:, 0, 0, :]
        PV = W[:, :, 1, :]
        Vb = sb("Vb", [P, BLK, D])
        S = sb("S", [P, BLK, HEADS])
        mask = sb("mask", [P, BLK])
        lim = sb("lim", [P, BLK])
        smax = sb("smax", [P, BLK, HEADS])
        ex = sb("ex", [P, BLK + 1, HEADS])
        pr = sb("pr", [P, BLK + 1, HEADS])
        mrun = sb("mrun", [P, HEADS])
        mnew = sb("mnew", [P, HEADS])
        mblk = sb("mblk", [P, HEADS])
        z = sb("z", [P, HEADS])
        zblk = sb("zblk", [P, HEADS])
        acc = sb("acc", [P, D])
        rest = sb("rest", [P, 1])
        alpha = pr[:, BLK, :]
        heads = lambda ap: ap.rearrange("p (d h) -> p d h", h=HEADS)

        block = nc.Block()
        with block:
            @block.sync
            def _(sp):
                load_records(sp, m, [(k_step, 2), (v_copied, 1)], last_group(sp))

            @block.gpsimd
            def _(pool):
                gather(pool, m, [(k_step, 2), (v_copied, 1)], kv_d, 2 * D, total_slots(pool))
                for t in range(NT):
                    pool.wait_ge(m.done, t + 1)
                    pool.indirect_dma_start(out, bass.IndirectOffsetOnAxis(ap=node[:, t, 0:1], axis=0), X[:, t, :],
                                            None, bounds_check=N - 1, oob_is_err=False).then_inc(m.stored, 16)
                pool.wait_ge(m.stored, 16 * NT)

            @block.tensor
            def _(pe):
                pe.sem_inc(m.used, WRING)
                blocks, end_r = pe.alloc_register("blocks_pe"), pe.alloc_register("end_pe")
                pe.reg_mov(blocks, 0)
                with pe.Fori(0, NT) as t:
                    lo, hi = tile_slots(pe, t)
                    with pe.Fori(lo, hi, BLK) as s0:
                        pe.wait_ge(added, pe.snap(blocks, min_val=0, max_val=E) + 1)
                        end = block_end(pe, end_r, s0, hi)
                        pe.matmul(agg[:, 0, 0:D], zrow[0:1, 0:P], zrow[0:1, 0:D], start=True, stop=False)
                        with pe.Fori(s0, end) as g:
                            pe.wait_ge(m.w_dve, g + 1)
                            pe.matmul(agg[:, 0, 0:D], ident, PV[:, g % WRING, :], start=False,
                                      stop=False).then_inc(m.used, 1)
                        pe.matmul(agg[:, 0, 0:D], zrow[0:1, 0:P], zrow[0:1, 0:D], start=False,
                                  stop=True).then_inc(m.agg_ready, 1)
                        pe.reg_add(blocks, blocks, 1)

            @block.scalar
            def _(act):
                act.preload_act_table(ACT.Exp)
                act.sem_inc(v_copied, RING)
                blocks, end_r = act.alloc_register("blocks_act"), act.alloc_register("end_act")
                act.reg_mov(blocks, 0)
                with act.Fori(0, NT) as t:
                    lo, hi = tile_slots(act, t)
                    with act.Fori(lo, hi, BLK) as s0:
                        end = block_end(act, end_r, s0, hi)
                        act.wait_ge(m.used, s0 + WRING)
                        with act.Fori(s0, end) as g:
                            act.wait_ge(m.arrived, g + 1)
                            act.nop(nofuse=True)
                            act.activation(Vb[:, place(g, s0), :], G[:, g % RING, D:2 * D], ACT.Copy).then_inc(v_copied, 1)
                        b = act.snap(blocks, min_val=0, max_val=E)
                        act.wait_ge(sm, b * STEPS + 7)
                        act.activation(pr[:], ex[:], ACT.Exp).then_inc(ex_done, 1)
                        act.reg_add(blocks, blocks, 1)
                deviation_all(act, m)

            @block.vector
            def _(dve):
                dve.sem_inc(k_step, 2 * RING)
                dve.sem_inc(added, 1)
                dve.sem_inc(m.ln, 1)
                dve.memset(S[:], 0.0).then_inc(m.tr_ready, 1)
                dve.wait_ge(m.tr_ready, 1)
                blocks, end_r = dve.alloc_register("blocks_dve"), dve.alloc_register("end_dve")
                dve.reg_mov(blocks, 0)
                with dve.Fori(0, NT) as t:
                    lo, hi = tile_slots(dve, t)
                    dve.wait_ge(m.ln, t * 2 + 1)
                    dve.memset(mrun[:], LOW)
                    dve.memset(z[:], 0.0)
                    dve.memset(acc[:], 0.0)
                    dve.tensor_copy(rest[:], node[:, bass.ds(t, 1), 2].bitcast(F32)).then_inc(fin, 1)
                    with dve.Fori(lo, hi, BLK) as s0:
                        end = block_end(dve, end_r, s0, hi)
                        with dve.Fori(s0, end) as g:
                            dve.wait_ge(m.arrived, g + 1)
                            dve.wait_ge(k_step, g * 2 + 2 * RING)
                            dve.tensor_tensor(prod, G[:, g % RING, 0:D], at(H, t), ALU.mult).then_inc(k_step, 1)
                            dve.wait_ge(k_step, g * 2 + 2 * RING + 1)
                            dve.nop(nofuse=True)
                            dve.tensor_reduce(S[:, place(g, s0), :], heads(prod).rearrange("p d h -> p h d"), AX_X,
                                              ALU.add).then_inc(k_step, 1)
                        b = dve.snap(blocks, min_val=0, max_val=E)
                        base = b * STEPS
                        dve.wait_ge(fin, t * FINS + 1)
                        dve.wait_ge(added, b + 1)
                        dve.tensor_scalar(mask[:], con[:, C_I32:C_I32 + BLK], rest[:], None, ALU.is_lt).then_inc(sm, 1)
                        dve.wait_ge(sm, base + 1)
                        dve.tensor_scalar(lim[:], mask[:], BIG, LOW, ALU.mult, ALU.add).then_inc(sm, 1)
                        dve.tensor_scalar(rest[:], rest[:], -float(BLK), None, ALU.add).then_inc(sm, 1)
                        dve.wait_ge(sm, base + 3)
                        dve.wait_ge(k_step, end * 2 + 2 * RING)
                        dve.tensor_tensor(smax[:], S[:], bc(lim[:], 2, HEADS), ALU.min).then_inc(sm, 1)
                        dve.wait_ge(sm, base + 4)
                        dve.nop(nofuse=True)
                        dve.tensor_reduce(mblk[:], smax[:].rearrange("p j h -> p h j"), AX_X, ALU.max).then_inc(sm, 1)
                        dve.wait_ge(sm, base + 5)
                        dve.tensor_tensor(mnew[:], mblk[:], mrun[:], ALU.max).then_inc(sm, 1)
                        dve.wait_ge(sm, base + 6)
                        dve.tensor_tensor(ex[:, BLK, :], mrun[:], mnew[:], ALU.subtract)
                        dve.tensor_tensor(ex[:, 0:BLK, :], smax[:], bc(mnew[:], 1, BLK), ALU.subtract).then_inc(sm, 1)
                        dve.wait_ge(ex_done, b + 1)
                        dve.tensor_copy(mrun[:], mnew[:]).then_inc(sm, 1)
                        dve.tensor_tensor(pr[:, 0:BLK, :], pr[:, 0:BLK, :], bc(mask[:], 2, HEADS), ALU.mult).then_inc(sm, 1)
                        dve.tensor_tensor(z[:], z[:], alpha, ALU.mult).then_inc(sm, 1)
                        dve.wait_ge(sm, base + 10)
                        dve.tensor_tensor(heads(acc[:]), heads(acc[:]), bc(alpha, 1, HD), ALU.mult).then_inc(sm, 1)
                        dve.nop(nofuse=True)
                        dve.tensor_reduce(zblk[:], pr[:, 0:BLK, :].rearrange("p j h -> p h j"), AX_X, ALU.add).then_inc(sm, 1)
                        dve.wait_ge(sm, base + 12)
                        dve.tensor_tensor(z[:], z[:], zblk[:], ALU.add).then_inc(sm, 1)
                        with dve.Fori(s0, end) as g:
                            dve.wait_ge(v_copied, g + 1 + RING)
                            dve.wait_ge(m.used, g + 1)
                            dve.tensor_tensor(heads(PV[:, g % WRING, :]), heads(Vb[:, place(g, s0), :]),
                                              bc(pr[:, place(g, s0), :], 1, HD), ALU.mult).then_inc(m.w_dve, 1)
                        dve.wait_ge(m.agg_ready, b + 1)
                        dve.wait_ge(sm, base + 13)
                        dve.tensor_tensor(acc[:], acc[:], agg[:, 0, 0:D], ALU.add).then_inc(added, 1)
                        dve.reg_add(blocks, blocks, 1)
                    b = dve.snap(blocks, min_val=0, max_val=E)
                    dve.wait_ge(added, b + 1)
                    dve.tensor_scalar(z[:], z[:], 1e-30, None, ALU.max).then_inc(fin, 1)
                    dve.wait_ge(fin, t * FINS + 2)
                    dve.reciprocal(z[:], z[:]).then_inc(fin, 1)
                    dve.wait_ge(fin, t * FINS + 3)
                    dve.tensor_tensor(heads(acc[:]), heads(acc[:]), bc(z[:], 1, HD), ALU.mult).then_inc(fin, 1)
                    dve.wait_ge(fin, t * FINS + 4)
                    residual(dve, m, t, lambda x: dve.tensor_tensor(x, acc[:], x, ALU.add))
                normalise_all(dve, m)

    s_x = sem("s_x")
    block = nc.Block()
    with block:
        @block.gpsimd
        def _(pool):
            for t in range(NT):
                pool.indirect_dma_start(X[:, t, :], None, h_d[0],
                                        bass.IndirectOffsetOnAxis(ap=node[:, t, 0:1], axis=0)).then_inc(s_x, 16)
            pool.wait_ge(s_x, 16 * NT)
    sum_layer(0, h_d[0], 2, F_C0, [w_bases[:, b, :] for b in range(2)], w_self[:], None, "res")
    if STOP > 1:
        sum_layer(1, h_d[1], 4, F_C1, [w_basis[:, 0, b, :] for b in range(4)], w_loop[:, 0, :], b_rows[:, 0:D], "tanh")
    if STOP > 2:
        sum_layer(2, h_d[2], 4, F_C2, [w_basis[:, 1, b, :] for b in range(4)], w_loop[:, 1, :], b_rows[:, D:2 * D],
                  "tanh_res")
    if STOP > 3:
        sum_layer(3, h_d[3], 1, F_OK, [w_lin[:]], None, b_rows[:, 2 * D:3 * D], "relu_res")
    if STOP > 4:
        attention_layer(4)


STOP = 9


def layout(i):
    import numpy as np

    f = lambda v: np.ascontiguousarray(np.asarray(v))
    edges = lambda v, fill: np.concatenate([f(v), np.full(EP - E, fill, np.int32)])
    dst = edges(i["dst"], PAD_DST)
    wrel = np.zeros((2, 64, 2, NCO), np.float32)
    for k in range(2):
        wrel[k, :R16, k, 0:2] = f(i["L0_gnn_base_weights"])
        for l in range(2):
            wrel[k, R16:R16 + R32, k, 2 + 4 * l:6 + 4 * l] = f(i["L1_gnn_comp"])[l]
    return {
        "x": np.concatenate([f(i["x"]), np.zeros((NP - N, D), np.float32)]),
        "dst": np.concatenate([dst.reshape(P, EC), np.append(dst[EC::EC], np.int32(PAD_DST))[:, None]], 1),
        "src": edges(i["src"], 0).reshape(P, EC),
        "t16": edges(i["edge_type_16"], 0).reshape(P, EC),
        "t32": edges(i["edge_type_32"], 0).reshape(P, EC),
        "wrel": wrel.reshape(P, 2 * NCO),
        "con": constants(),
        "w_self": f(i["L0_gnn_self_weight"]),
        "w_bases": f(f(i["L0_gnn_bases"]).transpose(1, 0, 2)),
        "w_basis": f(f(i["L1_gnn_basis"]).transpose(2, 0, 1, 3)),
        "w_loop": f(f(i["L1_gnn_loop_w"]).transpose(1, 0, 2)),
        "w_lin": f(f(i["L2_gnn_W"]).T),
        "w_qkv": np.concatenate([f(i[f"L3_gnn_W{c}"]) for c in "qkv"], 1),
        "b_rows": np.concatenate([f(i["L1_gnn_bias"]).reshape(-1), f(i["L2_gnn_b"])]
                                 + [f(i[f"L3_gnn_b{c}"]) for c in "qkv"])[None],
    }


def kernel(**inputs):
    import numpy as _np
    import concourse.bacc as _bacc
    from concourse import mybir as _mybir
    from concourse.bass_utils import run_bass_kernel_spmd as _run

    nc = _bacc.Bacc("TRN2", target_bir_lowering=False, num_devices=1)
    arrays = {f"in_{k}": v for k, v in layout(inputs).items()}
    aps = {k[3:]: nc.dram_tensor(k, v.shape, _mybir.dt.from_np(v.dtype), kind="ExternalInput").ap()
           for k, v in arrays.items()}
    out = nc.dram_tensor("out_x", (N, D), _mybir.dt.float32, kind="ExternalOutput").ap()
    program(nc, aps, out)
    r = _run(nc, [arrays], core_ids=[0])
    return r.results[0]["out_x"]
```
